# Optimizing a Trainium2 kernel written in Bass

```python
import numpy as np
import jax
import jax.numpy as jnp

def _softmax(x, axis=-1):
    return jax.nn.softmax(x, axis=axis)

def _gelu(x):
    return jax.nn.gelu(x, approximate=True)

def _silu(x):
    return jax.nn.silu(x)

def _sigmoid(x):
    return jax.nn.sigmoid(x)

def _layernorm(x, axis=-1, eps=1e-05):
    m = jnp.mean(x, axis=axis, keepdims=True)
    v = jnp.var(x, axis=axis, keepdims=True)
    return (x - m) / jnp.sqrt(v + eps)

def _scatter_add(tgt, idx, src, axis=0):
    return tgt.at[idx].add(src)

def _segment_sum(src, seg, n):
    return jax.ops.segment_sum(src, seg, n)
kernel_name = 'mk_adj_resnorm_d2_adj_r2_35a902'

def setup_inputs(seed: int=0):
    np.random.seed(seed)
    _w = jnp.asarray

    def _rec_inputs():
        import jax
        import jax.numpy as jnp
        _gk = jax.random.key(seed)
        x = 7.22e-05 + 1 * jax.random.normal(jax.random.fold_in(_gk, 1), (4096, 256), jnp.float32)
        _w = (1.0 + jnp.arange(4096, dtype=jnp.float32)) ** (-0.5)
        _w = _w / _w.mean()
        _pij = jnp.clip(0.00390625 * _w[:, None] * _w[None, :], 0.0, 1.0)
        _a = jax.random.uniform(jax.random.fold_in(_gk, 2), (4096, 4096)) < _pij
        _a = jnp.logical_or(_a, jnp.eye(4096, dtype=bool))
        _af = _a.astype(jnp.float32)
        _af = _af * jax.random.uniform(jax.random.fold_in(_gk, 3), (4096, 4096), jnp.float32, 0.05, 1)
        adj = _af
        return (x, adj)
    x, adj = _rec_inputs()

    def _L0_gnn_setup():
        import jax, jax.numpy as jnp
        import numpy as np
        N = 8192
        F_IN = 256
        F_OUT = 256
        key = jax.random.key(seed)
        k = jax.random.split(key, 6)
        h = jax.random.normal(k[0], (N, F_IN), dtype=jnp.float32)
        adj = jax.random.uniform(k[1], (N, N), dtype=jnp.float32)
        W_neigh = jax.random.normal(k[2], (F_OUT, F_IN), dtype=jnp.float32) * (1.0 / np.sqrt(F_IN))
        b_neigh = jax.random.normal(k[3], (F_OUT,), dtype=jnp.float32) * 0.01
        W_self = jax.random.normal(k[4], (F_OUT, F_IN), dtype=jnp.float32) * (1.0 / np.sqrt(F_IN))
        b_self = jax.random.normal(k[5], (F_OUT,), dtype=jnp.float32) * 0.01
        return {'h': h, 'adj': adj, 'W_neigh': W_neigh, 'b_neigh': b_neigh, 'W_self': W_self, 'b_self': b_self}
    _L0_gnn_all = _L0_gnn_setup()
    _L0_gnn_in = {k: v for k, v in _L0_gnn_all.items() if k in ('W_neigh', 'b_neigh', 'W_self', 'b_self')}
    del _L0_gnn_all

    def _L1_gnn_setup():
        import jax, jax.numpy as jnp
        import numpy as np
        N = 4096
        DIN = 256
        DOUT = 256
        key = jax.random.key(seed)
        k1, k2, k3 = jax.random.split(key, 3)
        x = jax.random.normal(k1, (N, DIN), dtype=jnp.float32)
        adj = jax.random.uniform(k2, (N, N), dtype=jnp.float32)
        W = jax.random.normal(k3, (DIN, DOUT), dtype=jnp.float32) * (1.0 / np.sqrt(DIN))
        b = jnp.zeros((DOUT,), dtype=jnp.float32)
        return {'x': x, 'adj': adj, 'W': W, 'b': b}
    _L1_gnn_all = _L1_gnn_setup()
    _L1_gnn_in = {k: v for k, v in _L1_gnn_all.items() if k in ('W', 'b')}
    del _L1_gnn_all
    return {'x': x, 'adj': adj, 'L0_gnn_W_neigh': _L0_gnn_in['W_neigh'], 'L0_gnn_b_neigh': _L0_gnn_in['b_neigh'], 'L0_gnn_W_self': _L0_gnn_in['W_self'], 'L0_gnn_b_self': _L0_gnn_in['b_self'], 'L1_gnn_W': _L1_gnn_in['W'], 'L1_gnn_b': _L1_gnn_in['b']}

def reference(x, adj, L0_gnn_W_neigh, L0_gnn_b_neigh, L0_gnn_W_self, L0_gnn_b_self, L1_gnn_W, L1_gnn_b):
    import jax
    import jax.numpy as jnp

    def _L0_gnn_ref(h, adj, W_neigh, b_neigh, W_self, b_self):
        import jax, jax.numpy as jnp
        import numpy as np
        N = 8192
        F_IN = 256
        F_OUT = 256
        deg = jnp.sum(adj, axis=1, keepdims=True) + 1e-05
        adj_norm = adj / deg
        h_neigh = adj_norm @ h
        out = h_neigh @ W_neigh.T + b_neigh + h @ W_self.T + b_self
        return jax.nn.relu(out)

    def _L1_gnn_ref(x, adj, W, b):
        import jax, jax.numpy as jnp
        import numpy as np
        N = 4096
        DIN = 256
        DOUT = 256
        rowsum = adj.sum(axis=1)
        d_inv_sqrt = jnp.where(rowsum > 0, rowsum ** (-0.5), 0.0)
        normalized_adj = d_inv_sqrt[:, None] * adj * d_inv_sqrt[None, :]
        support = normalized_adj @ x
        out = support @ W + b
        return jax.nn.relu(out)
    x = _layernorm(x + _L0_gnn_ref(x, adj, L0_gnn_W_neigh, L0_gnn_b_neigh, L0_gnn_W_self, L0_gnn_b_self), axis=-1)
    x = _layernorm(x + _L1_gnn_ref(x, adj, L1_gnn_W, L1_gnn_b), axis=-1)
    return x

_drawn_inputs = setup_inputs


def setup_inputs(seed=0):
    import zlib

    import numpy as np

    out = dict(_drawn_inputs(seed))
    spreads = {'L1_gnn_b': (0.0, 0.1)}
    factors = {'L0_gnn_b_neigh': 8.0, 'L0_gnn_b_self': 8.0}
    for name, (base, spread) in spreads.items():
        noise = np.random.default_rng([zlib.crc32(name.encode()), seed]).standard_normal(out[name].shape)
        drawn = base * np.exp(spread * noise) if base else spread * noise
        out[name] = jnp.asarray(drawn.astype(out[name].dtype))
    for name, factor in factors.items():
        out[name] = (out[name] * factor).astype(out[name].dtype)
    return out
```

```python
import numpy as np
import concourse.bass as bass
from concourse import mybir
from contextlib import ExitStack

N = 4096
F = 256
P = 128
FH = F // P
JT = N // P
IB = 512
NB = N // IB
TB = IB // P
UJ = 2
NU = JT // UJ
UW = UJ * IB
RING = 4
XC = 4
NXC = JT // XC
ZOWN = JT - TB
EPS_DEG = 1e-5
EPS_NORM = 1e-5
TINY = 1e-35


def build(nc, x_nat, xt_in, adj_in, wn_in, bn_in, ws_in, bs_in, w1_in, b1_in, out):
    f32 = mybir.dt.float32
    f32r = mybir.dt.float32r
    ALU = mybir.AluOpType
    ACT = mybir.ActivationFunctionType

    ctx = ExitStack()
    with ctx:
        def sb(name, shape, dt=f32):
            return ctx.enter_context(nc.sbuf_tensor(name, shape, dt))

        def sem(name):
            return ctx.enter_context(nc.semaphore(name))

        x1_dram = nc.dram_tensor("x1_scratch", [NB, TB, P, F], f32, kind="Internal").ap()

        xs = sb("xs", [P, JT, 2, F], f32r)
        zs = sb("zs", [P, ZOWN, 2, F], f32r)
        raw = sb("raw", [P, RING, UW])
        hi = sb("hi", [P, RING, UW], f32r)
        lo = sb("lo", [P, RING, UW], f32r)
        acc = sb("acc", [P, 2, UW])
        st_hi = sb("st_hi", [P, FH, IB], f32r)
        st_lo = sb("st_lo", [P, FH, IB], f32r)
        xt = sb("xt_sb", [P, FH, IB])
        wn = sb("wn_sb", [P, 2, FH, F], f32r)
        ws = sb("ws_sb", [P, FH, F])
        w1_hi, w1_lo = xs[:, TB], xs[:, TB + 1]
        res = sb("res", [P, TB, F])
        tt = sb("tt", [P, TB, F])
        bias0 = sb("bias0", [P, F])
        bias1 = sb("bias1", [P, F])
        bias_s = sb("bias_s", [P, F])
        ones = sb("ones", [P, 1])
        free_mark = sb("free_mark", [P, 1])
        root_in = sb("root_in", [P, 2 * TB])
        root = sb("root", [P, 2 * TB])
        inv_root = sb("inv_root", [P, 2 * TB])
        newton = sb("newton", [P, 2 * TB])
        rs = root_in[:, TB:2 * TB]
        rstd = inv_root[:, 0:TB]
        pos = sb("pos", [P, TB])
        rdeg = sb("rdeg", [P, TB])
        d_all = sb("d_all", [P, JT])
        d_cur = sb("d_cur", [P, TB])
        stats = sb("stats", [P, TB, 6])
        mv = sb("mv", [P, TB, 2])
        nmr = sb("nmr", [P, TB])

        ps_main = [ctx.enter_context(nc.psum_tensor(f"ps_main{i}", [P, FH, IB], f32)) for i in range(2)]
        ps_epi = ctx.enter_context(nc.psum_tensor("ps_epi", [P, TB, 2 * F], f32))

        raw_full = [sem(f"raw_full{s}") for s in range(RING)]
        x_full = [sem(f"x_full{s}") for s in range(2)]
        wn_full, w1_full, ws_full, bias_full = sem("wn_full"), sem("w1_full"), sem("ws_full"), sem("bias_full")
        xt_full, res_full = sem("xt_full"), sem("res_full")
        tt_stored = sem("tt_stored")
        ones_set = sem("ones_set")
        xh_ready, xl_ready = sem("xh_ready"), sem("xl_ready")
        wh_ready, wl_ready = sem("wh_ready"), sem("wl_ready")
        h_ready, l_ready, acc_done = sem("h_ready"), sem("l_ready"), sem("acc_done")
        unit_done = sem("unit_done")
        sth_ready, stl_ready = sem("sth_ready"), sem("stl_ready")
        rs_summed, rs_copied = sem("rs_summed"), sem("rs_copied")
        self_done, tile_done, tile_read = sem("self_done"), sem("tile_done"), sem("tile_read")
        root_ready, root_taken = sem("root_ready"), sem("root_taken")
        norm_ready = sem("norm_ready")
        d_ready = sem("d_ready")
        x1_ready, zh_ready, z_ready = sem("x1_ready"), sem("zh_ready"), sem("z_ready")
        dve_chain = sem("dve_chain")

        block = ctx.enter_context(nc.Block())

        def slot(u):
            return u % RING

        def is_last(e):
            return isinstance(e, int) and e == NB - 1

        def z_tile(t, e):
            if is_last(e):
                return xs[:, t:t + 1]
            return zs[:, bass.ds(e * TB + t, 1)]

        def moving_weight(layer, part, k):
            if layer == 0:
                return wn[:, part, k, :]
            return (w1_lo if part else w1_hi)[:, k, :]

        def stationary(layer, part, jt, f):
            if layer == 0:
                return xs[:, jt, part, f * P:(f + 1) * P]
            src = zs[:, jt] if jt < ZOWN else xs[:, jt - ZOWN]
            return src[:, part, f * P:(f + 1) * P]

        def layers(eng, one_block, last_epilogue):
            for layer in range(2):
                one_block(layer, 0, 0, None if layer == 0 else (0, NB - 1))
                with eng.Fori(1, NB - 1, 2) as b:
                    one_block(layer, b, 1, (layer, b - 1))
                    one_block(layer, b + 1, 0, (layer, b))
                one_block(layer, NB - 1, 1, (layer, NB - 2))
            last_epilogue((1, NB - 1))

        @block.sync
        def _(sp):
            def load_x(c):
                if c >= 2:
                    sp.wait_ge(xl_ready, c - 1)
                dst = (res, tt)[c % 2]
                sp.dma_start(dst[:, :, :], x_nat[c]).then_inc(x_full[c % 2], 16)

            def one_block(layer, b, parity, epi):
                g0 = b * NU + layer * NB * NU
                for u in range(NU):
                    if not (epi is None and u < RING):
                        sp.wait_ge(l_ready, g0 + (u - RING + 1))
                        if layer == 0:
                            sp.wait_ge(acc_done, g0 + (u - RING + 1))
                        elif epi[0] == 0 and u == 0:
                            sp.wait_ge(acc_done, NB * NU)
                    sp.dma_start(raw[:, slot(u), :], adj_in[b, u]).then_inc(raw_full[slot(u)], 16)
                    if epi is None:
                        if u % 2 == 0:
                            load_x(u // 2)
                        if u == 3:
                            sp.dma_start(xt[:, :, 0:F], wn_in).then_inc(wn_full, 16)
                            sp.dma_start(ws[:, :, :], ws_in).then_inc(ws_full, 16)
                            for dst, src in ((bias0, bn_in), (bias_s, bs_in), (bias1, b1_in)):
                                sp.dma_start(dst[:, :], src.rearrange("(a n) -> a n", a=1).to_broadcast([P, F]))\
                                  .then_inc(bias_full, 16)
                    elif u == 2:
                        load_epilogue(*epi)
                    elif u == 9 and epi[0] == 0 and is_last(epi[1]):
                        sp.wait_ge(self_done, NB)
                        sp.dma_start(xt[:, :, 0:F], w1_in).then_inc(w1_full, 16)

            def load_epilogue(layer, e):
                if layer == 0:
                    sp.wait_ge(wl_ready, 1)
                    sp.dma_start(xt[:, :, :], xt_in[e]).then_inc(xt_full, 16)
                    sp.wait_ge(xl_ready, NXC)
                if layer == 1:
                    sp.wait_ge(tt_stored, (NB + 1) * 16)
                rows = x_nat[e] if layer == 0 else x1_dram[e].rearrange("t p f -> p t f")
                sp.dma_start(res[:, :, :], rows).then_inc(res_full, 16)

            def last_epilogue(epi):
                load_epilogue(*epi)
                sp.wait_ge(tt_stored, (2 * NB + 1) * 16)

            layers(sp, one_block, last_epilogue)

        @block.gpsimd
        def _(pool):
            pool.memset(ones[:, :], 1.0).then_inc(ones_set, 1)
            pool.memset(free_mark[:, :], 0.0).then_inc(tt_stored, 16)

        @block.scalar
        def _(act):
            def epilogue(layer, e, v):
                n = e + layer * NB
                if v == 3:
                    act.wait_ge(unit_done, (n + 1) * NU)
                    ps = ps_main[parity_of[0]]
                    act.activation(st_hi[:, :, :], ps[:, :, :], ACT.Copy).then_inc(sth_ready, 1)
                if v == 10:
                    act.wait_ge(root_ready, n + 1)
                    m = 2 * TB if layer == 0 else TB
                    act.activation(root[:, 0:m], root_in[:, 0:m], ACT.Sqrt).then_inc(root_taken, 1)
                if v == 12:
                    act.wait_ge(norm_ready, n + 1)
                    for t in range(TB):
                        act.activation(tt[:, t, :], tt[:, t, :], ACT.Identity, bias=nmr[:, t:t + 1],
                                       scale=rstd[:, t:t + 1]).then_inc(x1_ready, 1)
                    act.wait_ge(x1_ready, (n + 1) * TB)
                    if layer == 0:
                        for t in range(TB):
                            act.activation(z_tile(t, e)[:, 0, 0, :], tt[:, t, :], ACT.Copy,
                                           scale=d_cur[:, t:t + 1]).then_inc(zh_ready, 1)
                        act.dma_start(x1_dram[e].rearrange("t p f -> p t f"), tt[:, :, :]).then_inc(tt_stored, 16)
                    else:
                        act.dma_start(out[e].rearrange("t p f -> p t f"), tt[:, :, :]).then_inc(tt_stored, 16)

            parity_of = [0]

            def one_block(layer, b, parity, epi):
                parity_of[0] = 1 - parity
                g0 = b * NU + layer * NB * NU
                k0 = b * (NU // RING) + layer * NB * (NU // RING)
                for u in range(NU):
                    if epi is None:
                        if u % 2 == 0:
                            c = u // 2
                            act.wait_ge(x_full[c % 2], 16 * (c // 2 + 1))
                            act.activation(xs[:, c * XC:(c + 1) * XC, 0, :], (res, tt)[c % 2][:, :, :],
                                           ACT.Copy).then_inc(xh_ready, 1)
                        if u == 5:
                            act.wait_ge(wn_full, 16)
                            act.activation(wn[:, 0], xt[:, :, 0:F], ACT.Copy).then_inc(wh_ready, 1)
                    else:
                        epilogue(*epi, u)
                        if epi[0] == 0 and is_last(epi[1]) and u == 11:
                            act.wait_ge(w1_full, 16)
                            act.activation(w1_hi, xt[:, :, 0:F], ACT.Copy).then_inc(wh_ready, 1)
                    act.wait_ge(raw_full[slot(u)], (k0 + (u // RING + 1)) * 16)
                    if not (epi is None and u < RING):
                        act.wait_ge(unit_done, g0 + (u - RING + 1))
                    act.activation(hi[:, slot(u), :], raw[:, slot(u), :], ACT.Copy).then_inc(h_ready, 1)

            def last_epilogue(epi):
                parity_of[0] = 1
                for v in range(NU):
                    epilogue(*epi, v)

            layers(act, one_block, last_epilogue)

        LINKS = (3 + 3 * TB + 5, 1 + 2 * TB + 5)

        @block.vector
        def _(dve):
            parity_of = [0]
            links = [0, 0]

            def link(ins):
                links[0] += 1
                ins.then_inc(dve_chain, 1)
                dve.wait_ge(dve_chain, links[1] + links[0])

            def epilogue(layer, e, v):
                n = e + layer * NB
                if v == 0:
                    links[0] = 0
                links[1] = e * LINKS[layer] + (NB * LINKS[0] if layer else 0)
                if v == 3:
                    dve.wait_ge(sth_ready, n + 1)
                    ps = ps_main[parity_of[0]]
                    dve.tensor_tensor(st_lo[:, :, :], ps[:, :, :], st_hi[:, :, :].bitcast(f32),
                                      ALU.subtract).then_inc(stl_ready, 1)
                if v == 4 and layer == 0:
                    dve.wait_ge(rs_summed, e + 1)
                    link(dve.tensor_copy(rs, ps_epi[:, TB - 1, 0:TB]))
                    link(dve.tensor_scalar(rdeg[:, :], rs, EPS_DEG, None, ALU.add))
                    link(dve.reciprocal(rdeg[:, :], rdeg[:, :]))
                    dve.tensor_scalar(pos[:, :], rs, 0.0, None, ALU.is_gt).then_inc(rs_copied, 1)
                    dve.tensor_scalar(rs, rs, TINY, None, ALU.max)
                if v == 4 and layer == 1:
                    link(dve.tensor_copy(d_cur[:, :], d_all[:, bass.ds(e * TB, TB)]))
                if 5 <= v < 5 + TB:
                    t = v - 5
                    dve.wait_ge(tile_done, n * TB + (t + 1))
                    if t == 0:
                        dve.wait_ge(tt_stored, (n + 1) * 16)
                    row, prod = tt[:, t, :], ps_epi[:, t]
                    if layer == 0:
                        link(dve.scalar_tensor_tensor(out=row, in0=prod[:, 0:F], scalar=rdeg[:, t:t + 1],
                                                      in1=bias0[:, :], op0=ALU.mult, op1=ALU.add))
                        dve.tensor_tensor(row, prod[:, F:2 * F], row, ALU.add).then_inc(tile_read, 1)
                        dve.wait_ge(tile_read, n * TB + (t + 1))
                    else:
                        dve.scalar_tensor_tensor(out=row, in0=prod[:, 0:F], scalar=d_cur[:, t:t + 1],
                                                 in1=bias1[:, :], op0=ALU.mult, op1=ALU.add)\
                           .then_inc(tile_read, 1)
                        dve.wait_ge(tile_read, n * TB + (t + 1))
                    if t == 0:
                        dve.wait_ge(res_full, (n + 1) * 16)
                    link(dve.scalar_tensor_tensor(out=row, in0=row, scalar=0.0, in1=res[:, t, :],
                                                  op0=ALU.max, op1=ALU.add))
                    link(dve.bn_stats(stats[:, t, :], row))
                if v == 9:
                    for t in range(TB):
                        last = dve.bn_aggr(mv[:, t, :], stats[:, t, :])
                    link(last)
                    dve.tensor_scalar(root_in[:, 0:TB], mv[:, :, 1], EPS_NORM, None, ALU.add)\
                       .then_inc(root_ready, 1)
                if v == 10:
                    m = 2 * TB if layer == 0 else TB
                    dve.wait_ge(root_taken, n + 1)
                    r, q, a = inv_root[:, 0:m], newton[:, 0:m], root_in[:, 0:m]
                    link(dve.reciprocal(r, root[:, 0:m]))
                    link(dve.scalar_tensor_tensor(out=q, in0=a, scalar=-0.5, in1=r, op0=ALU.mult, op1=ALU.mult))
                    link(dve.tensor_tensor(q, q, r, ALU.mult))
                    link(dve.scalar_tensor_tensor(out=r, in0=q, scalar=1.5, in1=r, op0=ALU.add, op1=ALU.mult))
                    if layer == 0:
                        r_sum = inv_root[:, TB:2 * TB]
                        dve.tensor_tensor(d_cur[:, :], r_sum, pos[:, :], ALU.mult).then_inc(d_ready, 1)
                        dve.tensor_tensor(d_all[:, bass.ds(e * TB, TB)], r_sum, pos[:, :], ALU.mult)
                    dve.scalar_tensor_tensor(out=nmr[:, :], in0=mv[:, :, 0], scalar=-1.0, in1=rstd,
                                             op0=ALU.mult, op1=ALU.mult).then_inc(norm_ready, 1)
                if v == 13 and layer == 0:
                    for t in range(TB):
                        dve.wait_ge(zh_ready, n * TB + (t + 1))
                        z = z_tile(t, e)
                        dve.scalar_tensor_tensor(out=z[:, 0, 1, :], in0=tt[:, t, :], scalar=d_cur[:, t:t + 1],
                                                 in1=z[:, 0, 0, :].bitcast(f32), op0=ALU.mult,
                                                 op1=ALU.subtract).then_inc(z_ready, 1)

            def one_block(layer, b, parity, epi):
                parity_of[0] = 1 - parity
                g0 = b * NU + layer * NB * NU
                for u in range(NU):
                    if epi is None:
                        if u % 2 == 0:
                            c = u // 2
                            dve.wait_ge(xh_ready, c + 1)
                            at = slice(c * XC, (c + 1) * XC)
                            dve.tensor_tensor(xs[:, at, 1, :], (res, tt)[c % 2][:, :, :],
                                              xs[:, at, 0, :].bitcast(f32), ALU.subtract).then_inc(xl_ready, 1)
                        if u == 5:
                            dve.wait_ge(wh_ready, 1)
                            dve.tensor_tensor(wn[:, 1], xt[:, :, 0:F], wn[:, 0].bitcast(f32),
                                              ALU.subtract).then_inc(wl_ready, 1)
                        if u == 7:
                            dve.wait_ge(bias_full, 48)
                            dve.tensor_tensor(bias0[:, :], bias0[:, :], bias_s[:, :], ALU.add)
                    else:
                        epilogue(*epi, u)
                        if epi[0] == 0 and is_last(epi[1]) and u == 11:
                            dve.wait_ge(wh_ready, 2)
                            dve.tensor_tensor(w1_lo, xt[:, :, 0:F], w1_hi.bitcast(f32),
                                              ALU.subtract).then_inc(wl_ready, 1)
                    dve.wait_ge(h_ready, g0 + (u + 1))
                    dve.tensor_tensor(lo[:, slot(u), :], raw[:, slot(u), :], hi[:, slot(u), :].bitcast(f32),
                                      ALU.subtract).then_inc(l_ready, 1)
                    if layer == 0:
                        a = acc[:, parity, :]
                        if u == 0:
                            dve.tensor_copy(a, raw[:, slot(u), :]).then_inc(acc_done, 1)
                        else:
                            dve.wait_ge(acc_done, g0 + u)
                            dve.tensor_tensor(a, a, raw[:, slot(u), :], ALU.add).then_inc(acc_done, 1)

            def last_epilogue(epi):
                parity_of[0] = 1
                for v in range(NU):
                    epilogue(*epi, v)

            layers(dve, one_block, last_epilogue)

        @block.tensor
        def _(pe):
            def epilogue(layer, e, u):
                n = e + layer * NB
                par = parity_of[0]
                if u == 0 and layer == 0:
                    pe.wait_ge(acc_done, (e + 1) * NU)
                    pe.wait_ge(ones_set, 1)
                    for t in range(TB):
                        for q in range(UJ):
                            at = q * IB + t * P
                            last = pe.matmul(ps_epi[:, TB - 1, t:t + 1], acc[:, par, at:at + P], ones[:, :],
                                             start=(q == 0), stop=(q == UJ - 1))
                    last.then_inc(rs_summed, 1)
                if 1 <= u < 1 + TB:
                    t = u - 1
                    if t == 0:
                        pe.wait_ge(stl_ready, n + 1)
                        if layer == 1:
                            pe.wait_ge(wl_ready, 2)
                        else:
                            pe.wait_ge(wl_ready, 1)
                            pe.wait_ge(ws_full, 16)
                            pe.wait_ge(xt_full, (e + 1) * 16)
                    if t == TB - 1 and layer == 0:
                        pe.wait_ge(rs_copied, e + 1)
                    rows = slice(t * P, (t + 1) * P)
                    if layer == 0:
                        for k in range(FH):
                            last = pe.matmul(ps_epi[:, t, F:2 * F], xt[:, k, rows], ws[:, k, :],
                                             start=(k == 0), stop=(k == FH - 1))
                        if t == TB - 1:
                            last.then_inc(self_done, 1)
                    passes = [(st_hi, 0), (st_hi, 1), (st_lo, 0)]
                    for k in range(FH):
                        for q, (st, part) in enumerate(passes):
                            last = pe.matmul(ps_epi[:, t, 0:F], st[:, k, rows], moving_weight(layer, part, k),
                                             start=(k == 0 and q == 0), stop=(k == FH - 1 and q == 2))
                    last.then_inc(tile_done, 1)

            parity_of = [0]

            def one_block(layer, b, parity, epi):
                parity_of[0] = 1 - parity
                g0 = b * NU + layer * NB * NU
                ps = ps_main[parity]
                for u in range(NU):
                    if epi is None and u % 2 == 0:
                        pe.wait_ge(xl_ready, u // 2 + 1)
                    if layer == 1 and epi[0] == 0:
                        pe.wait_ge(z_ready, UJ * (u + 1))
                    pe.wait_ge(l_ready, g0 + (u + 1))
                    for q in range(UJ):
                        jt = u * UJ + q
                        cols = slice(q * IB, (q + 1) * IB)
                        for f in range(FH):
                            for i, (part, mov) in enumerate(((0, hi), (0, lo), (1, hi))):
                                last = pe.matmul(ps[:, f, :], stationary(layer, part, jt, f), mov[:, slot(u), cols],
                                                 start=(jt == 0 and i == 0), stop=(jt == JT - 1 and i == 2))
                    last.then_inc(unit_done, 1)
                    if epi is not None:
                        epilogue(*epi, u)

            def last_epilogue(epi):
                parity_of[0] = 1
                for u in range(NU):
                    epilogue(*epi, u)

            layers(pe, one_block, last_epilogue)


def kernel(x, adj, L0_gnn_W_neigh, L0_gnn_b_neigh, L0_gnn_W_self, L0_gnn_b_self, L1_gnn_W, L1_gnn_b):
    import concourse.bacc as bacc
    from concourse.bass_utils import run_bass_kernel_spmd

    as_np = np.asarray
    x, adj = as_np(x), as_np(adj)

    def contraction_rows(w):
        return np.ascontiguousarray(w.reshape(FH, P, F).transpose(1, 0, 2))

    arrays = {
        "x_nat": np.ascontiguousarray(x.reshape(NB, TB, P, F).transpose(0, 2, 1, 3)),
        "xt": np.ascontiguousarray(x.T.reshape(FH, P, NB, IB).transpose(2, 1, 0, 3)),
        "adj_t": np.ascontiguousarray(adj.T.reshape(NU, UJ, P, NB, IB).transpose(3, 0, 2, 1, 4))
                   .reshape(NB, NU, P, UW),
        "wn": contraction_rows(as_np(L0_gnn_W_neigh).T),
        "bn": as_np(L0_gnn_b_neigh),
        "ws": contraction_rows(as_np(L0_gnn_W_self).T),
        "bs": as_np(L0_gnn_b_self),
        "w1": contraction_rows(as_np(L1_gnn_W)),
        "b1": as_np(L1_gnn_b),
    }
    nc = bacc.Bacc("TRN2", target_bir_lowering=False, num_devices=1)
    args = [nc.dram_tensor(name, a.shape, mybir.dt.from_np(a.dtype), kind="ExternalInput").ap()
            for name, a in arrays.items()]
    out = nc.dram_tensor("out", (NB, TB, P, F), mybir.dt.float32, kind="ExternalOutput").ap()
    build(nc, *args, out)
    r = run_bass_kernel_spmd(nc, [arrays], core_ids=[0])
    return r.results[0]["out"].reshape(N, F)
```

```python
import numpy as np
import concourse.bass as bass
from concourse import mybir
from contextlib import ExitStack

N = 4096
F = 256
P = 128
FH = F // P
JT = N // P
IB = 512
NB = N // IB
TB = IB // P
UJ = 2
NU = JT // UJ
UW = UJ * IB
RING = 4
XC = 4
NXC = JT // XC
ZOWN = JT - TB
EPS_DEG = 1e-5
EPS_NORM = 1e-5
TINY = 1e-35


def build(nc, x_nat, xt_in, adj_in, wn_in, bn_in, ws_in, bs_in, w1_in, b1_in, out):
    f32 = mybir.dt.float32
    f32r = mybir.dt.float32r
    ALU = mybir.AluOpType
    ACT = mybir.ActivationFunctionType

    ctx = ExitStack()
    with ctx:
        def sb(name, shape, dt=f32):
            return ctx.enter_context(nc.sbuf_tensor(name, shape, dt))

        def sem(name):
            return ctx.enter_context(nc.semaphore(name))

        x1_dram = nc.dram_tensor("x1_scratch", [NB, TB, P, F], f32, kind="Internal").ap()

        xs = sb("xs", [P, JT, 2, F], f32r)
        zs = sb("zs", [P, ZOWN, 2, F], f32r)
        raw = sb("raw", [P, RING, UW])
        hi = sb("hi", [P, RING, UW], f32r)
        lo = sb("lo", [P, RING, UW], f32r)
        acc = sb("acc", [P, 2, UW])
        st_hi = sb("st_hi", [P, FH, IB], f32r)
        st_lo = sb("st_lo", [P, FH, IB], f32r)
        xt = sb("xt_sb", [P, FH, IB])
        wn = sb("wn_sb", [P, 2, FH, F], f32r)
        ws = sb("ws_sb", [P, 2, FH, F], f32r)
        w1_hi, w1_lo = xs[:, TB], xs[:, TB + 1]
        res = sb("res", [P, TB, F])
        tt = sb("tt", [P, TB, F])
        bias0 = sb("bias0", [P, F])
        bias1 = sb("bias1", [P, F])
        bias_s = sb("bias_s", [P, F])
        ones = sb("ones", [P, 1])
        free_mark = sb("free_mark", [P, 1])
        root_in = sb("root_in", [P, 2 * TB])
        root = sb("root", [P, 2 * TB])
        inv_root = sb("inv_root", [P, 2 * TB])
        newton = sb("newton", [P, 2 * TB])
        rs = root_in[:, TB:2 * TB]
        rstd = inv_root[:, 0:TB]
        pos = sb("pos", [P, TB])
        rdeg = sb("rdeg", [P, TB])
        d_all = sb("d_all", [P, JT])
        d_cur = sb("d_cur", [P, TB])
        stats = sb("stats", [P, TB, 6])
        mv = sb("mv", [P, TB, 2])
        sums = sb("sums", [P, TB])
        nmean = sb("nmean", [P, TB])
        squares = sb("squares", [P, TB])
        nmr = sb("nmr", [P, TB])

        ps_main = [ctx.enter_context(nc.psum_tensor(f"ps_main{i}", [P, FH, IB], f32)) for i in range(2)]
        ps_epi = ctx.enter_context(nc.psum_tensor("ps_epi", [P, TB, 2 * F], f32))

        raw_full = [sem(f"raw_full{s}") for s in range(RING)]
        x_first_full, xh_first, xl_first = sem("x_first_full"), sem("xh_first"), sem("xl_first")
        x_full = [sem(f"x_full{s}") for s in range(2)]
        wn_full, ws_full, w1_full, bias_full = sem("wn_full"), sem("ws_full"), sem("w1_full"), sem("bias_full")
        xt_full, res_full = sem("xt_full"), sem("res_full")
        tt_stored = sem("tt_stored")
        ones_set = sem("ones_set")
        xh_ready, xl_ready = sem("xh_ready"), sem("xl_ready")
        wh_ready, wl_ready = sem("wh_ready"), sem("wl_ready")
        xth_ready, xtl_ready = sem("xth_ready"), sem("xtl_ready")
        h_ready, l_ready, acc_done = sem("h_ready"), sem("l_ready"), sem("acc_done")
        acc_folded = sem("acc_folded")
        unit_done = sem("unit_done")
        sth_ready, stl_ready = sem("sth_ready"), sem("stl_ready")
        rs_summed, rs_copied = sem("rs_summed"), sem("rs_copied")
        tile_done, tile_read = sem("tile_done"), sem("tile_read")
        root_ready, root_taken = sem("root_ready"), sem("root_taken")
        mean_ready, squares_ready = sem("mean_ready"), sem("squares_ready")
        norm_ready = sem("norm_ready")
        d_ready = sem("d_ready")
        x1_ready, zh_ready, z_ready = sem("x1_ready"), sem("zh_ready"), sem("z_ready")
        half_done, y_ready = sem("half_done"), sem("y_ready")
        dve_chain = sem("dve_chain")

        block = ctx.enter_context(nc.Block())

        def slot(u):
            return u % RING

        def is_last(e):
            return isinstance(e, int) and e == NB - 1

        def is_first(b):
            return isinstance(b, int) and b == 0

        def z_tile(t, e):
            if is_last(e):
                return xs[:, t:t + 1]
            return zs[:, bass.ds(e * TB + t, 1)]

        def moving_weight(layer, part, k):
            if layer == 0:
                return wn[:, part, k, :]
            return (w1_lo if part else w1_hi)[:, k, :]

        def stationary(layer, part, jt, f):
            if layer == 0:
                return xs[:, jt, part, f * P:(f + 1) * P]
            src = zs[:, jt] if jt < ZOWN else xs[:, jt - ZOWN]
            return src[:, part, f * P:(f + 1) * P]

        def layers(eng, one_block, last_epilogue):
            for layer in range(2):
                one_block(layer, 0, 0, None if layer == 0 else (0, NB - 1))
                with eng.Fori(1, NB - 1, 2) as b:
                    one_block(layer, b, 1, (layer, b - 1))
                    one_block(layer, b + 1, 0, (layer, b))
                one_block(layer, NB - 1, 1, (layer, NB - 2))
            last_epilogue((1, NB - 1))

        @block.sync
        def _(sp):
            def load_x(c):
                if c >= 2:
                    sp.wait_ge(xl_ready, c - 1)
                dst = (res, tt)[c % 2]
                sp.dma_start(dst[:, :, :], x_nat[c]).then_inc(x_full[c % 2], 16)

            def load_x_first():
                sp.dma_start(res[:, 0:UJ, :], x_nat[0, :, 0:UJ, :]).then_inc(x_first_full, 16)

            def load_weights():
                sp.dma_start(xt[:, :, 0:F], wn_in).then_inc(wn_full, 16)
                sp.dma_start(xt[:, :, F:2 * F], ws_in).then_inc(ws_full, 16)
                for dst, src in ((bias0, bn_in), (bias_s, bs_in), (bias1, b1_in)):
                    sp.dma_start(dst[:, :], src.rearrange("(a n) -> a n", a=1).to_broadcast([P, F]))\
                      .then_inc(bias_full, 16)

            def load_xt(b, u):
                if u != (6 if is_first(b) else 3):
                    return
                if is_first(b):
                    sp.wait_ge(wl_ready, 2)
                sp.dma_start(xt[:, :, :], xt_in[b]).then_inc(xt_full, 16)

            def load_residual(layer, e):
                if layer == 1:
                    sp.wait_ge(tt_stored, (NB + 1) * 16)
                rows = x_nat[e] if layer == 0 else x1_dram[e].rearrange("t p f -> p t f")
                sp.dma_start(res[:, :, :], rows).then_inc(res_full, 16)

            def one_block(layer, b, parity, epi):
                g0 = b * NU + layer * NB * NU
                for u in range(NU):
                    if epi is None and u == 0:
                        load_x_first()
                    if not (epi is None and u < RING):
                        sp.wait_ge(l_ready, g0 + (u - RING + 1))
                        if layer == 0 or (is_first(b) and u < RING):
                            sp.wait_ge(acc_done, g0 + (u - RING + 1))
                    sp.dma_start(raw[:, slot(u), :], adj_in[b, u]).then_inc(raw_full[slot(u)], 16)
                    if layer == 0:
                        load_xt(b, u)
                    if epi is None:
                        if u == 0:
                            sp.dma_start(res[:, UJ:XC, :], x_nat[0, :, UJ:XC, :]).then_inc(x_full[0], 16)
                        elif u % 2 == 1 and u < NU - 1:
                            load_x((u + 1) // 2)
                        if u == 2:
                            load_weights()
                    elif u == 2:
                        load_residual(*epi)
                        if layer == 1 and is_first(b):
                            sp.dma_start(xt[:, :, 0:F], w1_in).then_inc(w1_full, 16)

            def last_epilogue(epi):
                load_residual(*epi)
                for t in range(TB // 2):
                    sp.wait_ge(y_ready, t + 1)
                    sp.dma_start(out[NB - 1, t], tt[:, t, :]).then_inc(tt_stored, 16)
                sp.wait_ge(tt_stored, (2 * NB + TB) * 16)

            layers(sp, one_block, last_epilogue)

        @block.gpsimd
        def _(pool):
            pool.memset(ones[:, :], 1.0).then_inc(ones_set, 1)
            pool.memset(free_mark[:, :], 0.0).then_inc(tt_stored, 16)

        @block.scalar
        def _(act):
            def split_hi(dst, src):
                return act.activation(dst, src, ACT.Copy)

            def prologue(b, v):
                if v == 9:
                    act.wait_ge(xt_full, (b + 1) * 16)
                    if not is_first(b):
                        act.wait_ge(tile_done, b * TB)
                    split_hi(st_hi[:, :, :], xt[:, :, :]).then_inc(xth_ready, 1)

            def before_unit(n, parity, v):
                if v == 3:
                    act.wait_ge(unit_done, (n + 1) * NU)
                    split_hi(st_hi[:, :, :], ps_main[parity][:, :, :]).then_inc(sth_ready, 1)

            def square_tiles(n, pair):
                act.wait_ge(mean_ready, n * 2 + (pair + 1))
                for t in (2 * pair, 2 * pair + 1):
                    act.activation(ps_epi[:, t, 0:F], tt[:, t, :], ACT.Square, bias=nmean[:, t:t + 1],
                                   accum_out=squares[:, t:t + 1]).then_inc(squares_ready, 1)

            def norm_tile(n, t):
                if t == 0:
                    act.wait_ge(norm_ready, n + 1)
                act.activation(tt[:, t, :], tt[:, t, :], ACT.Identity, bias=nmr[:, t:t + 1],
                               scale=rstd[:, t:t + 1]).then_inc(x1_ready, 1)

            def z_hi(n, e, t):
                act.wait_ge(x1_ready, n * TB + (t + 1))
                act.activation(z_tile(t, e)[:, 0, 0, :], tt[:, t, :], ACT.Copy,
                               scale=d_cur[:, t:t + 1]).then_inc(zh_ready, 1)

            def after_unit(layer, e, v):
                n = e + layer * NB
                if v in (8, 10):
                    square_tiles(n, v // 2 - 4)
                if v == 11:
                    act.wait_ge(root_ready, n + 1)
                    m = 2 * TB if layer == 0 else TB
                    act.activation(root[:, 0:m], root_in[:, 0:m], ACT.Sqrt).then_inc(root_taken, 1)
                if v == 13:
                    norm_tile(n, 0)
                    norm_tile(n, 1)
                    if layer == 0:
                        z_hi(n, e, 0)
                if v == 14:
                    norm_tile(n, 2)
                    norm_tile(n, 3)
                    if layer == 0:
                        z_hi(n, e, 1)
                if v == 15:
                    if layer == 0:
                        z_hi(n, e, 2)
                        z_hi(n, e, 3)
                    act.wait_ge(x1_ready, (n + 1) * TB)
                    dst = (x1_dram if layer == 0 else out)[e]
                    act.dma_start(dst.rearrange("t p f -> p t f"), tt[:, :, :]).then_inc(tt_stored, 16)

            def one_block(layer, b, parity, epi):
                g0 = b * NU + layer * NB * NU
                k0 = b * (NU // RING) + layer * NB * (NU // RING)
                for u in range(NU):
                    if epi is None:
                        if u == 0:
                            act.wait_ge(x_first_full, 16)
                            split_hi(xs[:, 0:UJ, 0, :], res[:, 0:UJ, :]).then_inc(xh_first, 1)
                        elif u == 1 or u % 2 == 0:
                            c = u // 2
                            at = slice(c * XC if c else UJ, (c + 1) * XC)
                            rows = slice(0 if c else UJ, XC)
                            act.wait_ge(x_full[c % 2], 16 * (c // 2 + 1))
                            split_hi(xs[:, at, 0, :], (res, tt)[c % 2][:, rows, :]).then_inc(xh_ready, 1)
                        if u == 5:
                            act.wait_ge(wn_full, 16)
                            split_hi(wn[:, 0], xt[:, :, 0:F]).then_inc(wh_ready, 1)
                            act.wait_ge(ws_full, 16)
                            split_hi(ws[:, 0], xt[:, :, F:2 * F]).then_inc(wh_ready, 1)
                    else:
                        before_unit(epi[1] + epi[0] * NB, 1 - parity, u)
                        if layer == 1 and is_first(b) and u == 6:
                            act.wait_ge(w1_full, 16)
                            split_hi(w1_hi, xt[:, :, 0:F]).then_inc(wh_ready, 1)
                    if layer == 0:
                        prologue(b, u)
                    act.wait_ge(raw_full[slot(u)], (k0 + (u // RING + 1)) * 16)
                    if not (epi is None and u < RING):
                        act.wait_ge(unit_done, g0 + (u - RING + 1))
                    split_hi(hi[:, slot(u), :], raw[:, slot(u), :]).then_inc(h_ready, 1)
                    if epi is not None:
                        after_unit(*epi, u)

            def last_epilogue(epi):
                for f in range(FH):
                    act.wait_ge(half_done, f + 1)
                    split_hi(st_hi[:, f, :], ps_main[1][:, f, :]).then_inc(sth_ready, 1)
                act.wait_ge(root_ready, 2 * NB)
                act.activation(root[:, 0:TB], root_in[:, 0:TB], ACT.Sqrt).then_inc(root_taken, 1)
                act.wait_ge(norm_ready, 2 * NB)
                for t in range(TB // 2, TB):
                    act.activation(tt[:, t, :], tt[:, t, :], ACT.Identity, bias=nmr[:, t:t + 1],
                                   scale=rstd[:, t:t + 1]).then_inc(x1_ready, 1)
                for i, t in enumerate(range(TB // 2, TB)):
                    act.wait_ge(x1_ready, (2 * NB - 1) * TB + i + 1)
                    act.dma_start(out[NB - 1, t], tt[:, t, :]).then_inc(tt_stored, 16)

            layers(act, one_block, last_epilogue)

        LINKS = (4 + 2 * TB + 4, 1 + TB + 4)

        @block.vector
        def _(dve):
            links = [0, 0]

            def link(ins):
                links[0] += 1
                return ins.then_inc(dve_chain, 1)

            def linked(but=0):
                dve.wait_ge(dve_chain, links[1] + links[0] - but)

            def split_lo(dst, src, hi_part):
                return dve.tensor_tensor(dst, src, hi_part.bitcast(f32), ALU.subtract)

            def prologue(b, v, p):
                if (v, p) == (9, 1):
                    dve.wait_ge(xth_ready, b + 1)
                    split_lo(st_lo[:, :, :], xt[:, :, :], st_hi[:, :, :]).then_inc(xtl_ready, 1)

            def begin(layer, e):
                links[0], links[1] = 0, e * LINKS[layer] + (NB * LINKS[0] if layer else 0)

            def degrees(e, p):
                if p == 0:
                    dve.wait_ge(rs_summed, e + 1)
                    link(dve.tensor_copy(rs, ps_epi[:, TB - 1, 0:TB]))
                if p == 1:
                    linked()
                    link(dve.tensor_scalar(rdeg[:, :], rs, EPS_DEG, None, ALU.add))
                    dve.tensor_scalar(pos[:, :], rs, 0.0, None, ALU.is_gt).then_inc(rs_copied, 1)
                if p == 2:
                    linked()
                    link(dve.reciprocal(rdeg[:, :], rdeg[:, :]))
                    link(dve.tensor_scalar(rs, rs, TINY, None, ALU.max))

            def scale_product(layer, n, t):
                dve.wait_ge(tile_done, n * TB + (t + 1))
                if t == 0:
                    dve.wait_ge(tt_stored, (n + 1) * 16)
                    linked()
                ins = dve.scalar_tensor_tensor(
                    out=tt[:, t, :], in0=ps_epi[:, t, 0:F], scalar=(rdeg, d_cur)[layer][:, t:t + 1],
                    in1=(bias0, bias1)[layer][:, :], op0=ALU.mult, op1=ALU.add)
                if layer == 0:
                    link(ins)
                else:
                    ins.then_inc(tile_read, 1)

            def add_self(n, t):
                linked()
                dve.tensor_tensor(tt[:, t, :], ps_epi[:, t, F:2 * F], tt[:, t, :], ALU.add)\
                   .then_inc(tile_read, 1)

            def add_residual(n, t):
                if t == 0:
                    dve.wait_ge(res_full, (n + 1) * 16)
                dve.wait_ge(tile_read, n * TB + (t + 1))
                link(dve.scalar_tensor_tensor(out=tt[:, t, :], in0=tt[:, t, :], scalar=0.0, in1=res[:, t, :],
                                              op0=ALU.max, op1=ALU.add, accum_out=sums[:, t:t + 1]))

            def negate_means(pair):
                linked()
                at = slice(2 * pair, 2 * pair + 2)
                dve.tensor_scalar(nmean[:, at], sums[:, at], -1.0 / F, None, ALU.mult).then_inc(mean_ready, 1)

            def root_argument(n):
                dve.wait_ge(squares_ready, (n + 1) * TB)
                dve.tensor_scalar(root_in[:, 0:TB], squares[:, :], 1.0 / F, EPS_NORM, ALU.mult, ALU.add)\
                   .then_inc(root_ready, 1)

            def newton_step(layer, n, step):
                m = 2 * TB if layer == 0 else TB
                r, q, a = inv_root[:, 0:m], newton[:, 0:m], root_in[:, 0:m]
                if step == 0:
                    dve.wait_ge(root_taken, n + 1)
                    link(dve.reciprocal(r, root[:, 0:m]))
                if step == 1:
                    linked()
                    link(dve.scalar_tensor_tensor(out=q, in0=a, scalar=-0.5, in1=r, op0=ALU.mult, op1=ALU.mult))
                if step == 2:
                    linked()
                    link(dve.tensor_tensor(q, q, r, ALU.mult))
                if step == 3:
                    linked()
                    link(dve.scalar_tensor_tensor(out=r, in0=q, scalar=1.5, in1=r, op0=ALU.add, op1=ALU.mult))

            def norm_scales(layer, e):
                linked()
                if layer == 0:
                    r_sum = inv_root[:, TB:2 * TB]
                    dve.tensor_tensor(d_cur[:, :], r_sum, pos[:, :], ALU.mult).then_inc(d_ready, 1)
                    dve.tensor_tensor(d_all[:, bass.ds(e * TB, TB)], r_sum, pos[:, :], ALU.mult)
                dve.tensor_tensor(nmr[:, :], nmean[:, :], rstd, ALU.mult).then_inc(norm_ready, 1)

            def z_lo(n, e, t):
                dve.wait_ge(zh_ready, n * TB + (t + 1))
                z = z_tile(t, e)
                dve.scalar_tensor_tensor(out=z[:, 0, 1, :], in0=tt[:, t, :], scalar=d_cur[:, t:t + 1],
                                         in1=z[:, 0, 0, :].bitcast(f32), op0=ALU.mult,
                                         op1=ALU.subtract).then_inc(z_ready, 1)

            def epilogue(layer, e, parity, v, p):
                n = e + layer * NB
                if (v, p) == (0, 0):
                    begin(layer, e)
                if (v, p) == (0, 1) and layer == 0:
                    dve.wait_ge(acc_done, (e + 1) * NU)
                    a = acc[:, parity, :]
                    dve.tensor_tensor(a[:, 0:IB], a[:, 0:IB], a[:, IB:UW], ALU.add).then_inc(acc_folded, 1)
                if (v, p) == (3, 0):
                    dve.wait_ge(sth_ready, n + 1)
                    split_lo(st_lo[:, :, :], ps_main[parity][:, :, :], st_hi[:, :, :]).then_inc(stl_ready, 1)
                if v == 4 and layer == 0:
                    degrees(e, p)
                if (v, p) == (4, 0) and layer == 1:
                    link(dve.tensor_copy(d_cur[:, :], d_all[:, bass.ds(e * TB, TB)]))
                if 5 <= v < 5 + TB:
                    if p == 0:
                        scale_product(layer, n, v - 5)
                    if p == 1 and layer == 0:
                        add_self(n, v - 5)
                    if p == 2:
                        add_residual(n, v - 5)
                if v in (7, 9) and p == 1:
                    negate_means((v - 7) // 2)
                if (v, p) == (11, 0):
                    root_argument(n)
                if (v, p) == (11, 2):
                    newton_step(layer, n, 0)
                if v == 12:
                    newton_step(layer, n, p + 1)
                if (v, p) == (13, 0):
                    norm_scales(layer, e)
                if v == 15 and layer == 0:
                    z_lo(n, e, p)
                    if p == 2:
                        z_lo(n, e, 3)

            def one_block(layer, b, parity, epi):
                g0 = b * NU + layer * NB * NU

                def place(u, p):
                    if epi is not None:
                        epilogue(*epi, 1 - parity, u, p)
                    if layer == 0:
                        prologue(b, u, p)

                for u in range(NU):
                    if epi is None:
                        if u == 0:
                            dve.wait_ge(xh_first, 1)
                            split_lo(xs[:, 0:UJ, 1, :], res[:, 0:UJ, :], xs[:, 0:UJ, 0, :]).then_inc(xl_first, 1)
                        elif u == 1 or u % 2 == 0:
                            c = u // 2
                            at = slice(c * XC if c else UJ, (c + 1) * XC)
                            rows = slice(0 if c else UJ, XC)
                            dve.wait_ge(xh_ready, c + 1)
                            split_lo(xs[:, at, 1, :], (res, tt)[c % 2][:, rows, :], xs[:, at, 0, :])\
                                .then_inc(xl_ready, 1)
                        if u == 5:
                            for i, (w, cols) in enumerate(((wn, slice(0, F)), (ws, slice(F, 2 * F)))):
                                dve.wait_ge(wh_ready, i + 1)
                                split_lo(w[:, 1], xt[:, :, cols], w[:, 0]).then_inc(wl_ready, 1)
                        if u == 7:
                            dve.wait_ge(bias_full, 48)
                            dve.tensor_tensor(bias0[:, :], bias0[:, :], bias_s[:, :], ALU.add)
                    elif layer == 1 and is_first(b) and u == 6:
                        dve.wait_ge(wh_ready, 3)
                        split_lo(w1_lo, xt[:, :, 0:F], w1_hi).then_inc(wl_ready, 1)
                    place(u, 0)
                    dve.wait_ge(h_ready, g0 + (u + 1))
                    split_lo(lo[:, slot(u), :], raw[:, slot(u), :], hi[:, slot(u), :]).then_inc(l_ready, 1)
                    place(u, 1)
                    if layer == 0:
                        a = acc[:, parity, :]
                        if u == 0:
                            dve.tensor_copy(a, raw[:, slot(u), :]).then_inc(acc_done, 1)
                        else:
                            dve.wait_ge(acc_done, g0 + u)
                            dve.tensor_tensor(a, a, raw[:, slot(u), :], ALU.add).then_inc(acc_done, 1)
                    place(u, 2)
                assert epi is None or links[0] == LINKS[epi[0]], links

            def last_epilogue(epi):
                layer, e = epi
                n = e + layer * NB
                begin(layer, e)
                link(dve.tensor_copy(d_cur[:, :], d_all[:, e * TB:(e + 1) * TB]))
                for f in range(FH):
                    dve.wait_ge(sth_ready, n + 1 + f)
                    split_lo(st_lo[:, f, :], ps_main[1][:, f, :], st_hi[:, f, :]).then_inc(stl_ready, 1)
                for t in range(TB + 2):
                    if t < TB:
                        scale_product(layer, n, t)
                    if 1 <= t <= TB:
                        add_residual(n, t - 1)
                    if t >= 2:
                        linked(but=1)
                        link(dve.bn_stats(stats[:, t - 2, :], tt[:, t - 2, :]))
                linked()
                for t in range(TB):
                    last = dve.bn_aggr(mv[:, t, :], stats[:, t, :])
                link(last)
                linked()
                dve.tensor_scalar(root_in[:, 0:TB], mv[:, :, 1], EPS_NORM, None, ALU.add).then_inc(root_ready, 1)
                for step in range(4):
                    newton_step(layer, n, step)
                linked()
                dve.scalar_tensor_tensor(out=nmr[:, :], in0=mv[:, :, 0], scalar=-1.0, in1=rstd,
                                         op0=ALU.mult, op1=ALU.mult).then_inc(norm_ready, 1)
                dve.wait_ge(norm_ready, 2 * NB)
                for t in range(TB // 2):
                    dve.tensor_scalar(tt[:, t, :], tt[:, t, :], rstd[:, t:t + 1], nmr[:, t:t + 1],
                                      ALU.mult, ALU.add).then_inc(y_ready, 1)

            layers(dve, one_block, last_epilogue)

        @block.tensor
        def _(pe):
            def product(ps, rows, weight):
                passes = [(st_hi, 0), (st_hi, 1), (st_lo, 0)]
                for k in range(FH):
                    for q, (st, part) in enumerate(passes):
                        last = pe.matmul(ps, st[:, k, rows], weight(part, k),
                                         start=(k == 0 and q == 0), stop=(k == FH - 1 and q == 2))
                return last

            def prologue(b, u):
                if 9 <= u < 9 + TB:
                    t = u - 9
                    if t == 0:
                        pe.wait_ge(wl_ready, 2)
                        pe.wait_ge(xtl_ready, b + 1)
                    product(ps_epi[:, t, F:2 * F], slice(t * P, (t + 1) * P), lambda part, k: ws[:, part, k, :])

            def epilogue(layer, e, parity, u):
                n = e + layer * NB
                if u == 0 and layer == 0:
                    pe.wait_ge(acc_folded, e + 1)
                    pe.wait_ge(ones_set, 1)
                    for t in range(TB):
                        last = pe.matmul(ps_epi[:, TB - 1, t:t + 1], acc[:, parity, t * P:(t + 1) * P],
                                         ones[:, :], start=True, stop=True)
                    last.then_inc(rs_summed, 1)
                if 1 <= u < 1 + TB:
                    t = u - 1
                    if t == 0:
                        pe.wait_ge(stl_ready, n + 1)
                    if t == TB - 1 and layer == 0:
                        pe.wait_ge(rs_copied, e + 1)
                    product(ps_epi[:, t, 0:F], slice(t * P, (t + 1) * P),
                            lambda part, k: moving_weight(layer, part, k)).then_inc(tile_done, 1)

            def one_block(layer, b, parity, epi):
                g0 = b * NU + layer * NB * NU
                ps = ps_main[parity]
                for u in range(NU):
                    if epi is None:
                        if u == 0:
                            pe.wait_ge(xl_first, 1)
                        elif u == 1 or u % 2 == 0:
                            pe.wait_ge(xl_ready, u // 2 + 1)
                    if layer == 1 and epi[0] == 0:
                        pe.wait_ge(z_ready, UJ * (u + 1))
                    if layer == 1 and epi[0] == 1 and isinstance(epi[1], int) is False and u == 0:
                        pe.wait_ge(wl_ready, 3)
                    pe.wait_ge(l_ready, g0 + (u + 1))
                    ends = layer == 1 and is_last(b) and u == NU - 1
                    for f, q in [(f, q) for f in range(FH) for q in range(UJ)]:
                        jt = u * UJ + q
                        cols = slice(q * IB, (q + 1) * IB)
                        for i, (part, mov) in enumerate(((0, hi), (0, lo), (1, hi))):
                            last = pe.matmul(ps[:, f, :], stationary(layer, part, jt, f), mov[:, slot(u), cols],
                                             start=(jt == 0 and i == 0), stop=(jt == JT - 1 and i == 2))
                        if ends and q == UJ - 1:
                            last.then_inc(half_done, 1)
                    if not ends:
                        last.then_inc(unit_done, 1)
                    if epi is not None:
                        epilogue(*epi, 1 - parity, u)
                    if layer == 0:
                        prologue(b, u)

            def last_epilogue(epi):
                n = 2 * NB - 1
                for t in range(TB):
                    if t == 0:
                        pe.wait_ge(stl_ready, n + FH)
                    product(ps_epi[:, t, 0:F], slice(t * P, (t + 1) * P),
                            lambda part, k: moving_weight(1, part, k)).then_inc(tile_done, 1)

            layers(pe, one_block, last_epilogue)


def kernel(x, adj, L0_gnn_W_neigh, L0_gnn_b_neigh, L0_gnn_W_self, L0_gnn_b_self, L1_gnn_W, L1_gnn_b):
    import concourse.bacc as bacc
    from concourse.bass_utils import run_bass_kernel_spmd

    as_np = np.asarray
    x, adj = as_np(x), as_np(adj)

    def contraction_rows(w):
        return np.ascontiguousarray(w.reshape(FH, P, F).transpose(1, 0, 2))

    arrays = {
        "x_nat": np.ascontiguousarray(x.reshape(NB, TB, P, F).transpose(0, 2, 1, 3)),
        "xt": np.ascontiguousarray(x.T.reshape(FH, P, NB, IB).transpose(2, 1, 0, 3)),
        "adj_t": np.ascontiguousarray(adj.T.reshape(NU, UJ, P, NB, IB).transpose(3, 0, 2, 1, 4))
                   .reshape(NB, NU, P, UW),
        "wn": contraction_rows(as_np(L0_gnn_W_neigh).T),
        "bn": as_np(L0_gnn_b_neigh),
        "ws": contraction_rows(as_np(L0_gnn_W_self).T),
        "bs": as_np(L0_gnn_b_self),
        "w1": contraction_rows(as_np(L1_gnn_W)),
        "b1": as_np(L1_gnn_b),
    }
    nc = bacc.Bacc("TRN2", target_bir_lowering=False, num_devices=1)
    args = [nc.dram_tensor(name, a.shape, mybir.dt.from_np(a.dtype), kind="ExternalInput").ap()
            for name, a in arrays.items()]
    out = nc.dram_tensor("out", (NB, TB, P, F), mybir.dt.float32, kind="ExternalOutput").ap()
    build(nc, *args, out)
    r = run_bass_kernel_spmd(nc, [arrays], core_ids=[0])
    return r.results[0]["out"].reshape(N, F)
```

```python
import numpy as np
import concourse.bass as bass
from concourse import mybir
from contextlib import ExitStack

N = 4096
F = 256
P = 128
FH = F // P
JT = N // P
IB = 512
NB = N // IB
TB = IB // P
UJ = 2
NU = JT // UJ
UW = UJ * IB
RING = 4
XC = 4
WHOLE = XC // UJ
ZOWN = JT - TB
EPS_DEG = 1e-5
EPS_NORM = 1e-5
TINY = 1e-35


def build(nc, x_nat, xt_in, adj_in, wn_in, bn_in, ws_in, bs_in, w1_in, b1_in, out):
    f32 = mybir.dt.float32
    f32r = mybir.dt.float32r
    ALU = mybir.AluOpType
    ACT = mybir.ActivationFunctionType

    ctx = ExitStack()
    with ctx:
        def sb(name, shape, dt=f32):
            return ctx.enter_context(nc.sbuf_tensor(name, shape, dt))

        def sem(name):
            return ctx.enter_context(nc.semaphore(name))

        x1_dram = nc.dram_tensor("x1_scratch", [NB, TB, P, F], f32, kind="Internal").ap()

        xs = sb("xs", [P, JT, 2, F], f32r)
        zs = sb("zs", [P, ZOWN, 2, F], f32r)
        raw = sb("raw", [P, RING, UW])
        hi = sb("hi", [P, RING, UW], f32r)
        lo = sb("lo", [P, RING, UW], f32r)
        acc = sb("acc", [P, 2, UW])
        st_hi = sb("st_hi", [P, FH, IB], f32r)
        st_lo = sb("st_lo", [P, FH, IB], f32r)
        xt = sb("xt_sb", [P, FH, IB])
        wn = sb("wn_sb", [P, 2, FH, F], f32r)
        ws = sb("ws_sb", [P, 2, FH, F], f32r)
        w1_hi, w1_lo = xs[:, TB], xs[:, TB + 1]
        res = sb("res", [P, TB, F])
        tt = sb("tt", [P, TB, F])
        bias0 = sb("bias0", [P, F])
        bias1 = sb("bias1", [P, F])
        bias_s = sb("bias_s", [P, F])
        ones = sb("ones", [P, 1])
        marks = sb("marks", [P, 3])
        root_in = sb("root_in", [P, 2 * TB])
        root = sb("root", [P, 2 * TB])
        inv_root = sb("inv_root", [P, 2 * TB])
        newton = sb("newton", [P, 2 * TB])
        rstd = inv_root[:, 0:TB]
        pos = sb("pos", [P, TB])
        rdeg = sb("rdeg", [P, TB])
        d_all = sb("d_all", [P, JT])
        d_cur = sb("d_cur", [P, TB])
        stats = sb("stats", [P, TB, 6])
        mv = sb("mv", [P, TB, 2])
        sums = sb("sums", [P, TB])
        nmean = sb("nmean", [P, TB])
        squares = sb("squares", [P, TB])
        nmr = sb("nmr", [P, TB])

        ps_main = [ctx.enter_context(nc.psum_tensor(f"ps_main{i}", [P, FH, IB], f32)) for i in range(2)]
        ps_epi = ctx.enter_context(nc.psum_tensor("ps_epi", [P, TB, 2 * F], f32))

        raw_full = [sem(f"raw_full{s}") for s in range(RING)]
        x_first_full = [sem(f"x_first_full{u}") for u in range(WHOLE)]
        x_full = [sem(f"x_full{s}") for s in range(2)]
        wn_full, ws_full, w1_full, bias_full = sem("wn_full"), sem("ws_full"), sem("w1_full"), sem("bias_full")
        xt_full, res_full = sem("xt_full"), sem("res_full")
        tt_stored = sem("tt_stored")
        ones_set = sem("ones_set")
        xh_ready, xl_ready = sem("xh_ready"), sem("xl_ready")
        wh_ready, wl_ready = sem("wh_ready"), sem("wl_ready")
        xth_ready, xtl_ready = sem("xth_ready"), sem("xtl_ready")
        h_ready, l_ready, acc_done = sem("h_ready"), sem("l_ready"), sem("acc_done")
        acc_folded = sem("acc_folded")
        unit_done = sem("unit_done")
        sth_ready, stl_ready = sem("sth_ready"), sem("stl_ready")
        rs_summed, rs_copied = sem("rs_summed"), sem("rs_copied")
        tile_done, tile_read = sem("tile_done"), sem("tile_read")
        root_ready, root_taken = sem("root_ready"), sem("root_taken")
        mean_ready, squares_ready = sem("mean_ready"), sem("squares_ready")
        norm_ready = sem("norm_ready")
        x1_ready, zh_ready, z_ready = sem("x1_ready"), sem("zh_ready"), sem("z_ready")
        half_done, y_ready = sem("half_done"), sem("y_ready")
        dve_chain = sem("dve_chain")

        block = ctx.enter_context(nc.Block())

        def slot(u):
            return u % RING

        def is_last(e):
            return isinstance(e, int) and e == NB - 1

        def is_first(b):
            return isinstance(b, int) and b == 0

        def xt_unit(b):
            return 10 if is_first(b) else 9

        def x_stage(c):
            if c == 0:
                return acc[:, 1, :].rearrange("p (t f) -> p t f", t=XC)
            return (res, tt)[c % 2][:, :, :]

        def z_tile(t, e):
            if is_last(e):
                return xs[:, t:t + 1]
            return zs[:, bass.ds(e * TB + t, 1)]

        def moving_weight(layer, part, k):
            if layer == 0:
                return wn[:, part, k, :]
            return (w1_lo if part else w1_hi)[:, k, :]

        def stationary(layer, part, jt, f):
            if layer == 0:
                return xs[:, jt, part, f * P:(f + 1) * P]
            src = zs[:, jt] if jt < ZOWN else xs[:, jt - ZOWN]
            return src[:, part, f * P:(f + 1) * P]

        def layers(eng, one_block, last_epilogue):
            for layer in range(2):
                one_block(layer, 0, 0, None if layer == 0 else (0, NB - 1))
                with eng.Fori(1, NB - 1, 2) as b:
                    one_block(layer, b, 1, (layer, b - 1))
                    one_block(layer, b + 1, 0, (layer, b))
                one_block(layer, NB - 1, 1, (layer, NB - 2))
            last_epilogue((1, NB - 1))

        @block.sync
        def _(sp):
            def load_x(c):
                if c >= 3:
                    sp.wait_ge(xl_ready, c - 1)
                sp.dma_start(x_stage(c), x_nat[c]).then_inc(x_full[c % 2], 16)

            def load_x_first(half):
                at = slice(half * UJ, (half + 1) * UJ)
                sp.dma_start(x_stage(0)[:, at, :], x_nat[0, :, at, :]).then_inc(x_first_full[half], 16)

            def load_weights():
                sp.dma_start(xt[:, :, 0:F], wn_in).then_inc(wn_full, 16)
                sp.dma_start(xt[:, :, F:2 * F], ws_in).then_inc(ws_full, 16)
                for dst, src in ((bias0, bn_in), (bias_s, bs_in), (bias1, b1_in)):
                    sp.dma_start(dst[:, :], src.rearrange("(a n) -> a n", a=1).to_broadcast([P, F]))\
                      .then_inc(bias_full, 16)

            def load_xt(b, u):
                if u != (8 if is_first(b) else 3):
                    return
                if is_first(b):
                    sp.wait_ge(wl_ready, 2)
                sp.dma_start(xt[:, :, :], xt_in[b]).then_inc(xt_full, 16)

            def load_residual(layer, e):
                if layer == 1:
                    sp.wait_ge(tt_stored, (NB + 1) * 16)
                rows = x_nat[e] if layer == 0 else x1_dram[e].rearrange("t p f -> p t f")
                sp.dma_start(res[:, :, :], rows).then_inc(res_full, 16)

            def one_block(layer, b, parity, epi):
                g0 = b * NU + layer * NB * NU
                for u in range(NU):
                    if epi is None and u == 0:
                        load_x_first(0)
                    if not (epi is None and u < RING):
                        if epi is None and u - RING < WHOLE:
                            sp.wait_ge(unit_done, u - RING + 1)
                        else:
                            sp.wait_ge(l_ready, g0 + (u - RING + 1))
                        if layer == 0 or (is_first(b) and u < RING):
                            sp.wait_ge(acc_done, g0 + (u - RING + 1))
                    sp.dma_start(raw[:, slot(u), :], adj_in[b, u]).then_inc(raw_full[slot(u)], 16)
                    if layer == 0:
                        load_xt(b, u)
                    if epi is None:
                        if u == 0:
                            load_x_first(1)
                        elif u % 2 == 1 and u < NU - 1:
                            load_x((u + 1) // 2)
                        if u == 4:
                            load_weights()
                    elif u == 2:
                        load_residual(*epi)
                        if layer == 1 and is_first(b):
                            sp.dma_start(xt[:, :, 0:F], w1_in).then_inc(w1_full, 16)

            def last_epilogue(epi):
                load_residual(*epi)
                for t in range(TB // 2):
                    sp.wait_ge(y_ready, t + 1)
                    sp.dma_start(out[NB - 1, t], tt[:, t, :]).then_inc(tt_stored, 16)
                sp.wait_ge(tt_stored, (2 * NB + TB) * 16)

            layers(sp, one_block, last_epilogue)

        @block.gpsimd
        def _(pool):
            pool.memset(ones[:, :], 1.0).then_inc(ones_set, 1)
            pool.memset(marks[:, 0:1], 0.0).then_inc(tt_stored, 16)

        @block.scalar
        def _(act):
            def split_hi(dst, src):
                return act.activation(dst, src, ACT.Copy)

            def prologue(b, v):
                if v == xt_unit(b):
                    act.wait_ge(xt_full, (b + 1) * 16)
                    if not is_first(b):
                        act.wait_ge(tile_done, b * TB)
                    split_hi(st_hi[:, :, :], xt[:, :, :]).then_inc(xth_ready, 1)

            def before_unit(n, parity, v):
                if v == 3:
                    act.wait_ge(unit_done, (n + 1) * NU)
                    split_hi(st_hi[:, :, :], ps_main[parity][:, :, :]).then_inc(sth_ready, 1)

            def square_tiles(n, pair):
                act.wait_ge(mean_ready, n * 2 + (pair + 1))
                for t in (2 * pair, 2 * pair + 1):
                    act.activation(ps_epi[:, t, 0:F], tt[:, t, :], ACT.Square, bias=nmean[:, t:t + 1],
                                   accum_out=squares[:, t:t + 1]).then_inc(squares_ready, 1)

            def norm_tile(n, t):
                if t == 0:
                    act.wait_ge(norm_ready, n + 1)
                act.activation(tt[:, t, :], tt[:, t, :], ACT.Identity, bias=nmr[:, t:t + 1],
                               scale=rstd[:, t:t + 1]).then_inc(x1_ready, 1)

            def z_hi(n, e, t):
                act.wait_ge(x1_ready, n * TB + (t + 1))
                act.activation(z_tile(t, e)[:, 0, 0, :], tt[:, t, :], ACT.Copy,
                               scale=d_cur[:, t:t + 1]).then_inc(zh_ready, 1)

            def after_unit(layer, e, v):
                n = e + layer * NB
                if v in (8, 10):
                    square_tiles(n, v // 2 - 4)
                if v == 11:
                    act.wait_ge(root_ready, n + 1)
                    m = 2 * TB if layer == 0 else TB
                    act.activation(root[:, 0:m], root_in[:, 0:m], ACT.Sqrt).then_inc(root_taken, 1)
                if v == 13:
                    norm_tile(n, 0)
                    norm_tile(n, 1)
                    if layer == 0:
                        z_hi(n, e, 0)
                if v == 14:
                    norm_tile(n, 2)
                    norm_tile(n, 3)
                    if layer == 0:
                        z_hi(n, e, 1)
                if v == 15:
                    if layer == 0:
                        z_hi(n, e, 2)
                        z_hi(n, e, 3)
                    act.wait_ge(x1_ready, (n + 1) * TB)
                    dst = (x1_dram if layer == 0 else out)[e]
                    act.dma_start(dst.rearrange("t p f -> p t f"), tt[:, :, :]).then_inc(tt_stored, 16)

            def one_block(layer, b, parity, epi):
                g0 = b * NU + layer * NB * NU
                k0 = b * (NU // RING) + layer * NB * (NU // RING)
                for u in range(NU):
                    if epi is None:
                        if u % 2 == 0:
                            c = u // 2
                            if c == 0:
                                for full in x_first_full:
                                    act.wait_ge(full, 16)
                            else:
                                act.wait_ge(x_full[c % 2], 16 * ((c + 1) // 2))
                            split_hi(xs[:, c * XC:(c + 1) * XC, 0, :], x_stage(c)).then_inc(xh_ready, 1)
                        if u == 7:
                            act.wait_ge(wn_full, 16)
                            split_hi(wn[:, 0], xt[:, :, 0:F]).then_inc(wh_ready, 1)
                            act.wait_ge(ws_full, 16)
                            split_hi(ws[:, 0], xt[:, :, F:2 * F]).then_inc(wh_ready, 1)
                    else:
                        before_unit(epi[1] + epi[0] * NB, 1 - parity, u)
                        if layer == 1 and is_first(b) and u == 6:
                            act.wait_ge(w1_full, 16)
                            split_hi(w1_hi, xt[:, :, 0:F]).then_inc(wh_ready, 1)
                    if layer == 0:
                        prologue(b, u)
                    if epi is None and u < WHOLE:
                        continue
                    act.wait_ge(raw_full[slot(u)], (k0 + (u // RING + 1)) * 16)
                    if not (epi is None and u < RING):
                        act.wait_ge(unit_done, g0 + (u - RING + 1))
                    split_hi(hi[:, slot(u), :], raw[:, slot(u), :]).then_inc(h_ready, 1)
                    if epi is not None:
                        after_unit(*epi, u)

            def last_epilogue(epi):
                for f in range(FH):
                    act.wait_ge(half_done, f + 1)
                    split_hi(st_hi[:, f, :], ps_main[1][:, f, :]).then_inc(sth_ready, 1)
                act.wait_ge(root_ready, 2 * NB)
                act.activation(root[:, 0:TB], root_in[:, 0:TB], ACT.Sqrt).then_inc(root_taken, 1)
                act.wait_ge(norm_ready, 2 * NB)
                for t in range(TB // 2, TB):
                    act.activation(tt[:, t, :], tt[:, t, :], ACT.Identity, bias=nmr[:, t:t + 1],
                                   scale=rstd[:, t:t + 1]).then_inc(x1_ready, 1)
                for i, t in enumerate(range(TB // 2, TB)):
                    act.wait_ge(x1_ready, (2 * NB - 1) * TB + i + 1)
                    act.dma_start(out[NB - 1, t], tt[:, t, :]).then_inc(tt_stored, 16)

            act.wait_ge(ones_set, 1)
            act.activation(marks[:, 1:2], ones[:, :], ACT.Copy).then_inc(h_ready, WHOLE)
            layers(act, one_block, last_epilogue)

        LINKS = (2 + 2 * TB + 4, 1 + TB + 4)

        @block.vector
        def _(dve):
            links = [0, 0]

            def link(ins):
                links[0] += 1
                return ins.then_inc(dve_chain, 1)

            def linked(but=0):
                dve.wait_ge(dve_chain, links[1] + links[0] - but)

            def split_lo(dst, src, hi_part):
                return dve.tensor_tensor(dst, src, hi_part.bitcast(f32), ALU.subtract)

            def prologue(b, v, p):
                if (v, p) == (xt_unit(b), 1):
                    dve.wait_ge(xth_ready, b + 1)
                    split_lo(st_lo[:, :, :], xt[:, :, :], st_hi[:, :, :]).then_inc(xtl_ready, 1)

            def begin(layer, e):
                links[0], links[1] = 0, e * LINKS[layer] + (NB * LINKS[0] if layer else 0)

            def degrees(e, p):
                sums_of_rows = ps_epi[:, TB - 1, 0:TB]
                if p == 0:
                    dve.wait_ge(rs_summed, e + 1)
                    link(dve.tensor_scalar(rdeg[:, :], sums_of_rows, EPS_DEG, None, ALU.add))
                if p == 1:
                    dve.tensor_scalar(pos[:, :], sums_of_rows, 0.0, None, ALU.is_gt)
                    linked()
                    link(dve.reciprocal(rdeg[:, :], rdeg[:, :]))
                if p == 2:
                    dve.tensor_scalar(root_in[:, TB:2 * TB], sums_of_rows, TINY, None, ALU.max)\
                       .then_inc(rs_copied, 1)

            def scale_product(layer, n, t):
                dve.wait_ge(tile_done, n * TB + (t + 1))
                if t == 0:
                    dve.wait_ge(tt_stored, (n + 1) * 16)
                    linked()
                ins = dve.scalar_tensor_tensor(
                    out=tt[:, t, :], in0=ps_epi[:, t, 0:F], scalar=(rdeg, d_cur)[layer][:, t:t + 1],
                    in1=(bias0, bias1)[layer][:, :], op0=ALU.mult, op1=ALU.add)
                if layer == 0:
                    link(ins)
                else:
                    ins.then_inc(tile_read, 1)

            def add_self(n, t):
                linked()
                dve.tensor_tensor(tt[:, t, :], ps_epi[:, t, F:2 * F], tt[:, t, :], ALU.add)\
                   .then_inc(tile_read, 1)

            def add_residual(n, t):
                if t == 0:
                    dve.wait_ge(res_full, (n + 1) * 16)
                dve.wait_ge(tile_read, n * TB + (t + 1))
                link(dve.scalar_tensor_tensor(out=tt[:, t, :], in0=tt[:, t, :], scalar=0.0, in1=res[:, t, :],
                                              op0=ALU.max, op1=ALU.add, accum_out=sums[:, t:t + 1]))

            def negate_means(pair):
                linked()
                at = slice(2 * pair, 2 * pair + 2)
                dve.tensor_scalar(nmean[:, at], sums[:, at], -1.0 / F, None, ALU.mult).then_inc(mean_ready, 1)

            def root_argument(n):
                dve.wait_ge(squares_ready, (n + 1) * TB)
                dve.tensor_scalar(root_in[:, 0:TB], squares[:, :], 1.0 / F, EPS_NORM, ALU.mult, ALU.add)\
                   .then_inc(root_ready, 1)

            def newton_step(layer, n, step):
                m = 2 * TB if layer == 0 else TB
                r, q, a = inv_root[:, 0:m], newton[:, 0:m], root_in[:, 0:m]
                if step == 0:
                    dve.wait_ge(root_taken, n + 1)
                    link(dve.reciprocal(r, root[:, 0:m]))
                if step == 1:
                    linked()
                    link(dve.scalar_tensor_tensor(out=q, in0=a, scalar=-0.5, in1=r, op0=ALU.mult, op1=ALU.mult))
                if step == 2:
                    linked()
                    link(dve.tensor_tensor(q, q, r, ALU.mult))
                if step == 3:
                    linked()
                    link(dve.scalar_tensor_tensor(out=r, in0=q, scalar=1.5, in1=r, op0=ALU.add, op1=ALU.mult))

            def norm_scales(layer, e):
                linked()
                if layer == 0:
                    r_sum = inv_root[:, TB:2 * TB]
                    dve.tensor_tensor(d_cur[:, :], r_sum, pos[:, :], ALU.mult)
                    dve.tensor_tensor(d_all[:, bass.ds(e * TB, TB)], r_sum, pos[:, :], ALU.mult)
                dve.tensor_tensor(nmr[:, :], nmean[:, :], rstd, ALU.mult).then_inc(norm_ready, 1)

            def z_lo(n, e, t):
                dve.wait_ge(zh_ready, n * TB + (t + 1))
                z = z_tile(t, e)
                dve.scalar_tensor_tensor(out=z[:, 0, 1, :], in0=tt[:, t, :], scalar=d_cur[:, t:t + 1],
                                         in1=z[:, 0, 0, :].bitcast(f32), op0=ALU.mult,
                                         op1=ALU.subtract).then_inc(z_ready, 1)

            def epilogue(layer, e, parity, v, p):
                n = e + layer * NB
                if (v, p) == (0, 0):
                    begin(layer, e)
                if (v, p) == (0, 1) and layer == 0:
                    dve.wait_ge(acc_done, (e + 1) * NU)
                    a = acc[:, parity, :]
                    dve.tensor_tensor(a[:, 0:IB], a[:, 0:IB], a[:, IB:UW], ALU.add).then_inc(acc_folded, 1)
                if (v, p) == (3, 0):
                    dve.wait_ge(sth_ready, n + 1)
                    split_lo(st_lo[:, :, :], ps_main[parity][:, :, :], st_hi[:, :, :]).then_inc(stl_ready, 1)
                if v == 4 and layer == 0:
                    degrees(e, p)
                if (v, p) == (4, 0) and layer == 1:
                    link(dve.tensor_copy(d_cur[:, :], d_all[:, bass.ds(e * TB, TB)]))
                if 5 <= v < 5 + TB:
                    if p == 0:
                        scale_product(layer, n, v - 5)
                    if p == 1 and layer == 0:
                        add_self(n, v - 5)
                    if p == 2:
                        add_residual(n, v - 5)
                if v in (7, 9) and p == 1:
                    negate_means((v - 7) // 2)
                if (v, p) == (11, 0):
                    root_argument(n)
                if (v, p) == (11, 2):
                    newton_step(layer, n, 0)
                if v == 12:
                    newton_step(layer, n, p + 1)
                if (v, p) == (13, 0):
                    norm_scales(layer, e)
                if v == 15 and layer == 0:
                    z_lo(n, e, p)
                    if p == 2:
                        z_lo(n, e, 3)

            def one_block(layer, b, parity, epi):
                g0 = b * NU + layer * NB * NU

                def place(u, p):
                    if epi is not None:
                        epilogue(*epi, 1 - parity, u, p)
                    if layer == 0:
                        prologue(b, u, p)

                for u in range(NU):
                    if epi is None:
                        if u % 2 == 0:
                            c = u // 2
                            at = slice(c * XC, (c + 1) * XC)
                            dve.wait_ge(xh_ready, c + 1)
                            split_lo(xs[:, at, 1, :], x_stage(c), xs[:, at, 0, :]).then_inc(xl_ready, 1)
                        if u == 7:
                            for i, (w, cols) in enumerate(((wn, slice(0, F)), (ws, slice(F, 2 * F)))):
                                dve.wait_ge(wh_ready, i + 1)
                                split_lo(w[:, 1], xt[:, :, cols], w[:, 0]).then_inc(wl_ready, 1)
                        if u == 15:
                            dve.wait_ge(bias_full, 48)
                            dve.tensor_tensor(bias0[:, :], bias0[:, :], bias_s[:, :], ALU.add)
                    elif layer == 1 and is_first(b) and u == 6:
                        dve.wait_ge(wh_ready, 3)
                        split_lo(w1_lo, xt[:, :, 0:F], w1_hi).then_inc(wl_ready, 1)
                    place(u, 0)
                    if epi is None and u < WHOLE:
                        dve.wait_ge(raw_full[slot(u)], 16)
                    else:
                        dve.wait_ge(h_ready, g0 + (u + 1))
                        split_lo(lo[:, slot(u), :], raw[:, slot(u), :], hi[:, slot(u), :]).then_inc(l_ready, 1)
                    place(u, 1)
                    if layer == 0:
                        a = acc[:, parity, :]
                        if u == 1:
                            dve.tensor_tensor(a, raw[:, slot(0), :], raw[:, slot(1), :], ALU.add)\
                               .then_inc(acc_done, 2)
                        if u > 1:
                            dve.wait_ge(acc_done, g0 + u)
                            dve.tensor_tensor(a, a, raw[:, slot(u), :], ALU.add).then_inc(acc_done, 1)
                    place(u, 2)
                assert epi is None or links[0] == LINKS[epi[0]], links

            def last_epilogue(epi):
                layer, e = epi
                n = e + layer * NB
                begin(layer, e)
                link(dve.tensor_copy(d_cur[:, :], d_all[:, e * TB:(e + 1) * TB]))
                for f in range(FH):
                    dve.wait_ge(sth_ready, n + 1 + f)
                    split_lo(st_lo[:, f, :], ps_main[1][:, f, :], st_hi[:, f, :]).then_inc(stl_ready, 1)
                for t in range(TB + 2):
                    if t < TB:
                        scale_product(layer, n, t)
                    if 1 <= t <= TB:
                        add_residual(n, t - 1)
                    if t >= 2:
                        linked(but=1)
                        link(dve.bn_stats(stats[:, t - 2, :], tt[:, t - 2, :]))
                linked()
                for t in range(TB):
                    last = dve.bn_aggr(mv[:, t, :], stats[:, t, :])
                link(last)
                linked()
                dve.tensor_scalar(root_in[:, 0:TB], mv[:, :, 1], EPS_NORM, None, ALU.add).then_inc(root_ready, 1)
                for step in range(4):
                    newton_step(layer, n, step)
                linked()
                dve.scalar_tensor_tensor(out=nmr[:, :], in0=mv[:, :, 0], scalar=-1.0, in1=rstd,
                                         op0=ALU.mult, op1=ALU.mult).then_inc(norm_ready, 1)
                dve.wait_ge(norm_ready, 2 * NB)
                for t in range(TB // 2):
                    dve.tensor_scalar(tt[:, t, :], tt[:, t, :], rstd[:, t:t + 1], nmr[:, t:t + 1],
                                      ALU.mult, ALU.add).then_inc(y_ready, 1)

            dve.memset(marks[:, 2:3], 0.0).then_inc(l_ready, WHOLE)
            layers(dve, one_block, last_epilogue)

        @block.tensor
        def _(pe):
            def product(ps, rows, weight):
                passes = [(st_hi, 0), (st_hi, 1), (st_lo, 0)]
                for k in range(FH):
                    for q, (st, part) in enumerate(passes):
                        last = pe.matmul(ps, st[:, k, rows], weight(part, k),
                                         start=(k == 0 and q == 0), stop=(k == FH - 1 and q == 2))
                return last

            def prologue(b, u):
                t = u - xt_unit(b)
                if 0 <= t < TB:
                    if t == 0:
                        pe.wait_ge(wl_ready, 2)
                        pe.wait_ge(xtl_ready, b + 1)
                    product(ps_epi[:, t, F:2 * F], slice(t * P, (t + 1) * P), lambda part, k: ws[:, part, k, :])

            def epilogue(layer, e, parity, u):
                n = e + layer * NB
                if u == 0 and layer == 0:
                    pe.wait_ge(acc_folded, e + 1)
                    pe.wait_ge(ones_set, 1)
                    for t in range(TB):
                        last = pe.matmul(ps_epi[:, TB - 1, t:t + 1], acc[:, parity, t * P:(t + 1) * P],
                                         ones[:, :], start=True, stop=True)
                    last.then_inc(rs_summed, 1)
                if 1 <= u < 1 + TB:
                    t = u - 1
                    if t == 0:
                        pe.wait_ge(stl_ready, n + 1)
                    if t == TB - 1 and layer == 0:
                        pe.wait_ge(rs_copied, e + 1)
                    product(ps_epi[:, t, 0:F], slice(t * P, (t + 1) * P),
                            lambda part, k: moving_weight(layer, part, k)).then_inc(tile_done, 1)

            def one_block(layer, b, parity, epi):
                g0 = b * NU + layer * NB * NU
                ps = ps_main[parity]
                for u in range(NU):
                    if epi is None and u < WHOLE:
                        pe.wait_ge(x_first_full[u], 16)
                        pe.wait_ge(raw_full[slot(u)], 16)
                        for f, q in [(f, q) for f in range(FH) for q in range(UJ)]:
                            jt = u * UJ + q
                            last = pe.matmul(ps[:, f, :], x_stage(0)[:, jt, f * P:(f + 1) * P],
                                             raw[:, slot(u), q * IB:(q + 1) * IB], start=(jt == 0), stop=False)
                        last.then_inc(unit_done, 1)
                        continue
                    if epi is None and u % 2 == 0:
                        pe.wait_ge(xl_ready, u // 2 + 1)
                    if layer == 1 and epi[0] == 0:
                        pe.wait_ge(z_ready, UJ * (u + 1))
                    if layer == 1 and epi[0] == 1 and u == 0:
                        pe.wait_ge(wl_ready, 3)
                    pe.wait_ge(l_ready, g0 + (u + 1))
                    ends = layer == 1 and is_last(b) and u == NU - 1
                    for f, q in [(f, q) for f in range(FH) for q in range(UJ)]:
                        jt = u * UJ + q
                        cols = slice(q * IB, (q + 1) * IB)
                        for i, (part, mov) in enumerate(((0, hi), (0, lo), (1, hi))):
                            last = pe.matmul(ps[:, f, :], stationary(layer, part, jt, f), mov[:, slot(u), cols],
                                             start=(jt == 0 and i == 0), stop=(jt == JT - 1 and i == 2))
                        if ends and q == UJ - 1:
                            last.then_inc(half_done, 1)
                    if not ends:
                        last.then_inc(unit_done, 1)
                    if epi is not None:
                        epilogue(*epi, 1 - parity, u)
                    if layer == 0:
                        prologue(b, u)

            def last_epilogue(epi):
                n = 2 * NB - 1
                passes = [(st_hi, 0), (st_hi, 1), (st_lo, 0)]
                for k in range(FH):
                    pe.wait_ge(stl_ready, n + 1 + k)
                    for t in range(TB):
                        for q, (st, part) in enumerate(passes):
                            last = pe.matmul(ps_epi[:, t, 0:F], st[:, k, t * P:(t + 1) * P],
                                             moving_weight(1, part, k),
                                             start=(k == 0 and q == 0), stop=(k == FH - 1 and q == 2))
                        if k == FH - 1:
                            last.then_inc(tile_done, 1)

            layers(pe, one_block, last_epilogue)


def kernel(x, adj, L0_gnn_W_neigh, L0_gnn_b_neigh, L0_gnn_W_self, L0_gnn_b_self, L1_gnn_W, L1_gnn_b):
    import concourse.bacc as bacc
    from concourse.bass_utils import run_bass_kernel_spmd

    as_np = np.asarray
    x, adj = as_np(x), as_np(adj)

    def contraction_rows(w):
        return np.ascontiguousarray(w.reshape(FH, P, F).transpose(1, 0, 2))

    arrays = {
        "x_nat": np.ascontiguousarray(x.reshape(NB, TB, P, F).transpose(0, 2, 1, 3)),
        "xt": np.ascontiguousarray(x.T.reshape(FH, P, NB, IB).transpose(2, 1, 0, 3)),
        "adj_t": np.ascontiguousarray(adj.T.reshape(NU, UJ, P, NB, IB).transpose(3, 0, 2, 1, 4))
                   .reshape(NB, NU, P, UW),
        "wn": contraction_rows(as_np(L0_gnn_W_neigh).T),
        "bn": as_np(L0_gnn_b_neigh),
        "ws": contraction_rows(as_np(L0_gnn_W_self).T),
        "bs": as_np(L0_gnn_b_self),
        "w1": contraction_rows(as_np(L1_gnn_W)),
        "b1": as_np(L1_gnn_b),
    }
    nc = bacc.Bacc("TRN2", target_bir_lowering=False, num_devices=1)
    args = [nc.dram_tensor(name, a.shape, mybir.dt.from_np(a.dtype), kind="ExternalInput").ap()
            for name, a in arrays.items()]
    out = nc.dram_tensor("out", (NB, TB, P, F), mybir.dt.float32, kind="ExternalOutput").ap()
    build(nc, *args, out)
    r = run_bass_kernel_spmd(nc, [arrays], core_ids=[0])
    return r.results[0]["out"].reshape(N, F)
```
